# Optimizing a Trainium2 kernel written in Bass

```python
import numpy as np
import jax
import jax.numpy as jnp

def _softmax(x, axis=-1):
    return jax.nn.softmax(x, axis=axis)

def _gelu(x):
    return jax.nn.gelu(x, approximate=True)

def _silu(x):
    return jax.nn.silu(x)

def _sigmoid(x):
    return jax.nn.sigmoid(x)

def _layernorm(x, axis=-1, eps=1e-05):
    m = jnp.mean(x, axis=axis, keepdims=True)
    v = jnp.var(x, axis=axis, keepdims=True)
    return (x - m) / jnp.sqrt(v + eps)

def _scatter_add(tgt, idx, src, axis=0):
    return tgt.at[idx].add(src)

def _segment_sum(src, seg, n):
    return jax.ops.segment_sum(src, seg, n)
kernel_name = 'mk_recurrent_d2_jaxref_r8_05c400'

def setup_inputs(seed: int=0):
    np.random.seed(seed)
    _w = jnp.asarray

    def _L0_attn_setup():
        import jax, jax.numpy as jnp
        import numpy as np
        D_MODEL, D_QKV, N_HEADS = (128, 64, 16)
        key = jax.random.key(seed)
        k_x, k_qkv, k_out = jax.random.split(key, 3)
        X = jax.random.normal(k_x, (2, 256, D_MODEL), dtype=jnp.float32)
        W_qkv = jax.random.normal(k_qkv, (D_MODEL, 3 * D_QKV * N_HEADS), dtype=jnp.float32) * D_MODEL ** (-0.5)
        W_out = jax.random.normal(k_out, (D_QKV * N_HEADS, D_MODEL), dtype=jnp.float32) * (D_QKV * N_HEADS) ** (-0.5)
        return {'X': X, 'W_qkv': W_qkv, 'W_out': W_out}
    _L0_attn_in = _L0_attn_setup()

    def _L0_ffn_setup():
        import jax, jax.numpy as jnp
        import numpy as np
        TOP_K = 2

        def _mlp(x, w_fc, w_proj):
            return jnp.square(jax.nn.relu(x @ w_fc.T)) @ w_proj.T
        key = jax.random.key(seed)
        ks = jax.random.split(key, 6)
        B, S, D, E = (4, 256, 128, 8)
        d_ff = 4 * D
        x = jax.random.normal(ks[0], (B, S, D), dtype=jnp.float32)
        router_w = jax.random.normal(ks[1], (E, D), dtype=jnp.float32) * 0.02
        w_fc = jax.random.normal(ks[2], (E, d_ff, D), dtype=jnp.float32) * 0.02
        w_proj = jax.random.normal(ks[3], (E, D, d_ff), dtype=jnp.float32) * 0.02
        shared_fc = jax.random.normal(ks[4], (d_ff, D), dtype=jnp.float32) * 0.02
        shared_proj = jax.random.normal(ks[5], (D, d_ff), dtype=jnp.float32) * 0.02
        return {'x': x, 'router_w': router_w, 'w_fc': w_fc, 'w_proj': w_proj, 'shared_fc': shared_fc, 'shared_proj': shared_proj}
    _L0_ffn_in = _L0_ffn_setup()

    def _L1_attn_setup():
        import jax, jax.numpy as jnp
        import numpy as np
        EPS = 1e-06

        def _rmsnorm(x, w):
            x32 = x.astype(jnp.float32)
            n = x32 * jax.lax.rsqrt(jnp.mean(x32 * x32, axis=-1, keepdims=True) + EPS)
            return n.astype(x.dtype) * w

        def _reference_tuple_inner(u, dt, A, Bmat, C, D, norm_w):
            u = _rmsnorm(u, norm_w)
            Bsz, T, _ = u.shape
            dts = jax.nn.sigmoid(dt)
            a = jnp.exp(-dts * jnp.abs(A))
            t = jnp.arange(T, dtype=jnp.float32)
            h = dts[:, None] * a[:, None] ** t[None, :]
            u_proj = jnp.einsum('bti,is->bst', u, Bmat)
            k = jnp.flip(h, axis=1)[:, None, :]
            x = jax.lax.conv_general_dilated(u_proj, k, window_strides=(1,), padding=[(T - 1, T - 1)], dimension_numbers=('NCW', 'OIW', 'NCW'), feature_group_count=u_proj.shape[1])[:, :, :T]
            x = jnp.transpose(x, (0, 2, 1))
            y = jnp.einsum('bts,so->bto', x, C) + D
            return (y, x[:, -1])
        key = jax.random.key(seed)
        ks = jax.random.split(key, 8)
        I, S, O = (128, 64, 128)
        Bsz, T = (4, 256)
        return {'u': jax.random.normal(ks[0], (Bsz, T, I), dtype=jnp.float32), 'dt': jax.random.normal(ks[1], (S,), dtype=jnp.float32), 'A': jax.random.normal(ks[2], (S,), dtype=jnp.float32), 'Bmat': jax.random.normal(ks[3], (I, S), dtype=jnp.float32) / np.sqrt(S), 'C': jax.random.normal(ks[4], (S, O), dtype=jnp.float32) / np.sqrt(S), 'D': jax.random.normal(ks[5], (O,), dtype=jnp.float32), 'norm_w': jnp.ones((I,), dtype=jnp.float32)}
    _L1_attn_in = _L1_attn_setup()

    def _L1_ffn_setup():
        import jax, jax.numpy as jnp
        import numpy as np
        BLOCK = 16
        _GRID = jnp.array([0.0, 0.5, 1.0, 1.5, 2.0, 3.0, 4.0, 6.0], dtype=jnp.float32)
        _MID = jnp.array([0.25, 0.75, 1.25, 1.75, 2.5, 3.5, 5.0], dtype=jnp.float32)

        def fp4_quant_dequant(x):
            shape = x.shape
            xb = x.reshape(shape[:-1] + (shape[-1] // BLOCK, BLOCK))
            scale = jnp.max(jnp.abs(xb), axis=-1, keepdims=True) / 6.0
            scale = jnp.maximum(scale, jnp.float32(1e-12))
            xn = xb / scale
            idx = jnp.searchsorted(_MID, jnp.abs(xn))
            q = _GRID[idx] * jnp.sign(xn) * scale
            return q.reshape(shape)

        def fp4_linear(x, w):
            xq = fp4_quant_dequant(x)
            wq = fp4_quant_dequant(w)
            return jnp.einsum('bsk,nk->bsn', xq, wq)
        key = jax.random.key(seed)
        k1, k2, k3, k4 = jax.random.split(key, 4)
        H, I = (128, 352)
        x = jax.random.normal(k1, (4, 512, H), dtype=jnp.float32)
        w_gate = jax.random.normal(k2, (I, H), dtype=jnp.float32) * 0.02
        w_up = jax.random.normal(k3, (I, H), dtype=jnp.float32) * 0.02
        w_down = jax.random.normal(k4, (H, I), dtype=jnp.float32) * 0.02
        return {'x': x, 'w_gate': w_gate, 'w_up': w_up, 'w_down': w_down}
    _L1_ffn_in = _L1_ffn_setup()
    _d = {'L0_attn_X': _L0_attn_in['X'], 'L0_attn_W_qkv': _L0_attn_in['W_qkv'], 'L0_attn_W_out': _L0_attn_in['W_out'], 'L0_ffn_router_w': _L0_ffn_in['router_w'], 'L0_ffn_w_fc': _L0_ffn_in['w_fc'], 'L0_ffn_w_proj': _L0_ffn_in['w_proj'], 'L0_ffn_shared_fc': _L0_ffn_in['shared_fc'], 'L0_ffn_shared_proj': _L0_ffn_in['shared_proj'], 'L1_attn_dt': _L1_attn_in['dt'], 'L1_attn_A': _L1_attn_in['A'], 'L1_attn_Bmat': _L1_attn_in['Bmat'], 'L1_attn_C': _L1_attn_in['C'], 'L1_attn_D': _L1_attn_in['D'], 'L1_attn_norm_w': _L1_attn_in['norm_w'], 'L1_ffn_w_gate': _L1_ffn_in['w_gate'], 'L1_ffn_w_up': _L1_ffn_in['w_up'], 'L1_ffn_w_down': _L1_ffn_in['w_down']}
    _x0 = _d['L0_attn_X']
    _d['L0_attn_X'] = jax.random.normal(jax.random.fold_in(jax.random.key(seed), 1), (4, 1024, 128), dtype=_x0.dtype)
    del _x0
    return _d

def reference(L0_attn_X, L0_attn_W_qkv, L0_attn_W_out, L0_ffn_router_w, L0_ffn_w_fc, L0_ffn_w_proj, L0_ffn_shared_fc, L0_ffn_shared_proj, L1_attn_dt, L1_attn_A, L1_attn_Bmat, L1_attn_C, L1_attn_D, L1_attn_norm_w, L1_ffn_w_gate, L1_ffn_w_up, L1_ffn_w_down):

    def _L0_attn_ref(X, W_qkv, W_out):
        import jax, jax.numpy as jnp
        import numpy as np
        D_MODEL, D_QKV, N_HEADS = (128, 64, 16)
        b, s, _ = X.shape
        h, d = (N_HEADS, D_QKV)
        scale = d ** 0.5
        qkv = X @ W_qkv
        qkv = qkv.reshape(b, s, h, d, 3)
        q, k, v = (qkv[..., 0], qkv[..., 1], qkv[..., 2])
        scores = jnp.einsum('bqhd,bkhd->bhqk', q, k) / scale
        weights = jax.nn.softmax(scores, axis=-1)
        attn = jnp.einsum('bhqk,bkhd->bqhd', weights, v)
        return attn.reshape(b, s, h * d) @ W_out

    def _L0_ffn_ref(x, router_w, w_fc, w_proj, shared_fc, shared_proj):
        import jax, jax.numpy as jnp
        import numpy as np
        TOP_K = 2

        def _mlp(x, w_fc, w_proj):
            return jnp.square(jax.nn.relu(x @ w_fc.T)) @ w_proj.T
        B, S, D = x.shape
        E = router_w.shape[0]
        T = B * S
        flat = x.reshape(T, D)
        logits = flat @ router_w.T
        probs = jax.nn.softmax(logits.astype(jnp.float32), axis=-1)
        topk_p, topk_i = jax.lax.top_k(probs, TOP_K)
        topk_w = (topk_p / jnp.maximum(topk_p.sum(-1, keepdims=True), 1e-09)).astype(flat.dtype)
        combine = jnp.zeros((T, E), dtype=flat.dtype)
        combine = combine.at[jnp.arange(T)[:, None], topk_i].add(topk_w)
        out = jnp.zeros_like(flat)
        for e in range(E):
            out = out + _mlp(flat, w_fc[e], w_proj[e]) * combine[:, e:e + 1]
        out = out + _mlp(flat, shared_fc, shared_proj)
        return out.reshape(B, S, D)

    def _L1_attn_ref(u, dt, A, Bmat, C, D, norm_w):
        import jax, jax.numpy as jnp
        import numpy as np
        EPS = 1e-06

        def _rmsnorm(x, w):
            x32 = x.astype(jnp.float32)
            n = x32 * jax.lax.rsqrt(jnp.mean(x32 * x32, axis=-1, keepdims=True) + EPS)
            return n.astype(x.dtype) * w

        def _reference_tuple_inner(u, dt, A, Bmat, C, D, norm_w):
            u = _rmsnorm(u, norm_w)
            Bsz, T, _ = u.shape
            dts = jax.nn.sigmoid(dt)
            a = jnp.exp(-dts * jnp.abs(A))
            t = jnp.arange(T, dtype=jnp.float32)
            h = dts[:, None] * a[:, None] ** t[None, :]
            u_proj = jnp.einsum('bti,is->bst', u, Bmat)
            k = jnp.flip(h, axis=1)[:, None, :]
            x = jax.lax.conv_general_dilated(u_proj, k, window_strides=(1,), padding=[(T - 1, T - 1)], dimension_numbers=('NCW', 'OIW', 'NCW'), feature_group_count=u_proj.shape[1])[:, :, :T]
            x = jnp.transpose(x, (0, 2, 1))
            y = jnp.einsum('bts,so->bto', x, C) + D
            return (y, x[:, -1])
        return _reference_tuple_inner(u, dt, A, Bmat, C, D, norm_w)[0]

    def _L1_ffn_ref(x, w_gate, w_up, w_down):
        import jax, jax.numpy as jnp
        import numpy as np
        BLOCK = 16
        _GRID = jnp.array([0.0, 0.5, 1.0, 1.5, 2.0, 3.0, 4.0, 6.0], dtype=jnp.float32)
        _MID = jnp.array([0.25, 0.75, 1.25, 1.75, 2.5, 3.5, 5.0], dtype=jnp.float32)

        def fp4_quant_dequant(x):
            shape = x.shape
            xb = x.reshape(shape[:-1] + (shape[-1] // BLOCK, BLOCK))
            scale = jnp.max(jnp.abs(xb), axis=-1, keepdims=True) / 6.0
            scale = jnp.maximum(scale, jnp.float32(1e-12))
            xn = xb / scale
            idx = jnp.searchsorted(_MID, jnp.abs(xn))
            q = _GRID[idx] * jnp.sign(xn) * scale
            return q.reshape(shape)

        def fp4_linear(x, w):
            xq = fp4_quant_dequant(x)
            wq = fp4_quant_dequant(w)
            return jnp.einsum('bsk,nk->bsn', xq, wq)
        gate = fp4_linear(x, w_gate)
        y = fp4_linear(x, w_up)
        h = jax.nn.silu(gate) * y
        return fp4_linear(h, w_down)
    x = L0_attn_X
    xn = _layernorm(x, axis=-1)
    s = _L0_attn_ref(xn, L0_attn_W_qkv, L0_attn_W_out)
    g = _silu(_L0_ffn_ref(xn, L0_ffn_router_w, L0_ffn_w_fc, L0_ffn_w_proj, L0_ffn_shared_fc, L0_ffn_shared_proj))
    x = x + s * g
    xn = _layernorm(x, axis=-1)
    s = _L1_attn_ref(xn, L1_attn_dt, L1_attn_A, L1_attn_Bmat, L1_attn_C, L1_attn_D, L1_attn_norm_w)
    g = _silu(_L1_ffn_ref(xn, L1_ffn_w_gate, L1_ffn_w_up, L1_ffn_w_down))
    x = x + s * g
    return x

_drawn_inputs = setup_inputs


def setup_inputs(seed=0):
    import zlib

    import numpy as np

    out = dict(_drawn_inputs(seed))
    spreads = {'L1_attn_norm_w': (1.0, 0.6)}
    factors = {'L0_attn_W_qkv': 8.0,
     'L0_attn_W_out': 8.0,
     'L0_ffn_router_w': 8.0,
     'L0_ffn_w_fc': 8.0,
     'L0_ffn_w_proj': 8.0,
     'L0_ffn_shared_fc': 8.0,
     'L0_ffn_shared_proj': 8.0,
     'L1_attn_dt': 8.0,
     'L1_attn_A': 8.0,
     'L1_attn_Bmat': 7.215,
     'L1_attn_C': 7.166,
     'L1_attn_D': 25.246,
     'L1_ffn_w_gate': 5.873,
     'L1_ffn_w_up': 5.74,
     'L1_ffn_w_down': 5.748}
    for name, (base, spread) in spreads.items():
        noise = np.random.default_rng([zlib.crc32(name.encode()), seed]).standard_normal(out[name].shape)
        drawn = base * np.exp(spread * noise) if base else spread * noise
        out[name] = jnp.asarray(drawn.astype(out[name].dtype))
    for name, factor in factors.items():
        out[name] = (out[name] * factor).astype(out[name].dtype)
    return out
```

```python
import concourse.bass as bass
from concourse import mybir
from contextlib import ExitStack

F32 = mybir.dt.float32
F32R = mybir.dt.float32r
U32 = mybir.dt.uint32
ALU = mybir.AluOpType
ACT = mybir.ActivationFunctionType
AX = mybir.AxisListType

B, T, D = 4, 1024, 128
NT = B * T
P = 128
TILES = NT // P
TPB = T // P
CH = 512
NCH = NT // CH
H, DH = 16, 64
PAIRS = H // 2
E, FF = 8, 512
NE = E + 1
FT = FF // P
S = 64
INNER = 352
IB = [(0, 128), (128, 128), (256, 96)]
BLK = 16
LN_EPS = 1e-5
RMS_EPS = 1e-6


def layer0_norm_and_router(nc, ctx, g):
    sb, pb, sem = g.scope(ctx)
    x_tok = sb("x_tok", [P, TILES, D], F32)
    sq = sb("ln_sq", [P, 2, TPB, D], F32)
    sums = sb("ln_sums", [P, B, TPB], F32)
    neg_mean = sb("ln_neg_mean", [P, B, TPB], F32)
    var = sb("ln_var", [P, B, TPB], F32)
    rstd = sb("ln_rstd", [P, B, TPB], F32)
    mhalf = sb("ln_mhalf", [P, TPB], F32)
    rw_raw = sb("rw_raw", [P, E], F32)
    rw_hi = sb("rw_hi", [P, E], F32R)
    rw_lo = sb("rw_lo", [P, E], F32R)
    logits = sb("logits", [P, TILES, E], F32)
    top = sb("top", [P, TILES, 8], F32)
    top_i = sb("top_i", [P, TILES, 8], U32)
    top_f = sb("top_f", [P, TILES, 2], F32)
    gap = sb("gap", [P, TILES], F32)
    ratio = sb("ratio", [P, TILES], F32)
    w1 = sb("w1", [P, TILES], F32)
    w2 = sb("w2", [P, TILES], F32)
    pick = sb("pick", [P, TILES, E], F32)
    pick2 = sb("pick2", [P, TILES, E], F32)
    comb = sb("comb", [P, TILES, NE], F32)
    comb_hl = sb("comb_hl", [P, TILES, 2 * NE], F32R)
    iota8 = sb("iota8", [P, E], F32)
    ps_t = [pb(f"ps_t{i}", [P, TPB * P]) for i in range(2)]
    ps_lg = pb("ps_lg", [P, TILES * E])
    ps_c = pb("ps_c", [P, 2 * CH])

    x_in = [sem(f"x_in{b}") for b in range(B)]
    consts_in = sem("consts_in")
    dve = sem("ln_dve")
    sq_done = sem("sq_done")
    rstd_done = sem("rstd_done")
    xt_ready = sem("xt_ready")
    hi_done = sem("hi_done")
    lo_done = sem("lo_done")
    rw_done = sem("rw_done")
    lg_ready = sem("lg_ready")
    gap_done = sem("gap_done")
    ratio_done = sem("ratio_done")
    comb_done = sem("comb_done")
    ct_ready = sem("ct_ready")
    ct_done = sem("ct_done")
    xn_done = sem("xn_done")
    mh_done = sem("mh_done")

    with nc.Block() as block:
        @block.sync
        def _(sp):
            for b in range(B):
                sp.dma_start(x_tok[:, b * TPB:(b + 1) * TPB, :],
                             g.inp["X"][b].rearrange("(n p) d -> p n d", p=P)).then_inc(x_in[b], 16)
                if b == 0:
                    sp.dma_start(g.ident[:, :], g.inp["ident_d"]).then_inc(consts_in, 16)
                    sp.dma_start(rw_raw[:, :], g.inp["router_wT"]).then_inc(consts_in, 16)
                    sp.dma_start(iota8[:, :], g.inp["iota8_d"]).then_inc(consts_in, 16)

        @block.gpsimd
        def _(pool):
            nc.gpsimd.memset(mhalf[:, :], -0.5).then_inc(mh_done, 1)
            pool.wait_ge(mh_done, 1)
            for b in range(B):
                pool.wait_ge(dve, 5 * b + 5)
                nc.gpsimd.tensor_tensor(rstd[:, b, :], var[:, b, :], mhalf[:, :], ALU.pow).then_inc(rstd_done, 1)

        @block.scalar
        def _(act):
            for b in range(B):
                act.wait_ge(dve, 5 * b + 3)
                nc.scalar.activation(sq[:, b % 2], x_tok[:, b * TPB:(b + 1) * TPB, :],
                                     ACT.Square).then_inc(sq_done, 1)
                if b:
                    act.wait_ge(xt_ready, b)
                    nc.scalar.activation(g.xh[:, (b - 1) * T:b * T], ps_t[(b - 1) % 2][:, :],
                                         ACT.Copy).then_inc(hi_done, 1)
            act.wait_ge(xt_ready, B)
            nc.scalar.activation(g.xh[:, (B - 1) * T:B * T], ps_t[(B - 1) % 2][:, :], ACT.Copy).then_inc(hi_done, 1)
            act.wait_ge(gap_done, 1)
            nc.scalar.activation(ratio[:, :], gap[:, :], ACT.Exp).then_inc(ratio_done, 1)
            for q in range(TILES // 8):
                act.wait_ge(ct_ready, q + 1)
                nc.scalar.activation(g.combT[:, q * 2 * CH:(q + 1) * 2 * CH], ps_c[0:2 * NE, :],
                                     ACT.Copy).then_inc(ct_done, 1)

        @block.vector
        def _(v):
            v.wait_ge(consts_in, 48)
            nc.vector.tensor_copy(rw_hi[:, :], rw_raw[:, :]).then_inc(rw_done, 1)
            v.wait_ge(rw_done, 1)
            nc.vector.tensor_tensor(rw_lo[:, :], rw_raw[:, :], rw_hi[:, :].bitcast(F32),
                                    ALU.subtract).then_inc(rw_done, 1)

            def lo(b):
                v.wait_ge(hi_done, b + 1)
                nc.vector.tensor_tensor(g.xl[:, b * T:(b + 1) * T], ps_t[b % 2][:, :],
                                        g.xh[:, b * T:(b + 1) * T].bitcast(F32), ALU.subtract).then_inc(lo_done, 1)

            for b in range(B):
                x = x_tok[:, b * TPB:(b + 1) * TPB, :]
                v.wait_ge(x_in[b], 16)
                nc.vector.tensor_reduce(sums[:, b, :], x, AX.X, ALU.add).then_inc(dve, 1)
                v.wait_ge(dve, 5 * b + 1)
                nc.vector.tensor_scalar(neg_mean[:, b, :], sums[:, b, :], -1.0 / D, None, ALU.mult).then_inc(dve, 1)
                v.wait_ge(dve, 5 * b + 2)
                nc.vector.tensor_tensor(x, x, neg_mean[:, b, :].unsqueeze(2).to_broadcast([P, TPB, D]),
                                        ALU.add).then_inc(dve, 1)
                if b:
                    lo(b - 1)
                v.wait_ge(sq_done, b + 1)
                nc.vector.tensor_reduce(sums[:, b, :], sq[:, b % 2], AX.X, ALU.add).then_inc(dve, 1)
                v.wait_ge(dve, 5 * b + 4)
                nc.vector.tensor_scalar(var[:, b, :], sums[:, b, :], 1.0 / D, LN_EPS,
                                        ALU.mult, ALU.add).then_inc(dve, 1)
                v.wait_ge(rstd_done, b + 1)
                nc.vector.tensor_tensor(x, x, rstd[:, b, :].unsqueeze(2).to_broadcast([P, TPB, D]),
                                        ALU.mult).then_inc(xn_done, 1)
            lo(B - 1)
            n = 0

            def step(ins):
                nonlocal n
                n += 1
                ins.then_inc(comb_done, 1)
                v.wait_ge(comb_done, n)

            v.wait_ge(lg_ready, 1)
            step(nc.vector.tensor_copy(logits[:, :, :].rearrange("p n e -> p (n e)"), ps_lg[:, :]))
            for t in range(TILES):
                ins = nc.vector.max(top[:, t, :], logits[:, t, :])
            step(ins)
            for t in range(TILES):
                ins = nc.vector.max_index(top_i[:, t, :], top[:, t, :], logits[:, t, :])
            step(ins)
            step(nc.vector.tensor_copy(top_f[:, :, :], top_i[:, :, 0:2]))
            nc.vector.tensor_tensor(gap[:, :], top[:, :, 1], top[:, :, 0], ALU.subtract).then_inc(gap_done, 1)
            v.wait_ge(ratio_done, 1)
            step(nc.vector.tensor_scalar(gap[:, :], ratio[:, :], 1.0, None, ALU.add))
            step(nc.vector.reciprocal(w1[:, :], gap[:, :]))
            step(nc.vector.tensor_tensor(w2[:, :], w1[:, :], ratio[:, :], ALU.mult))
            io = iota8[:, :].unsqueeze(1).to_broadcast([P, TILES, E])
            step(nc.vector.tensor_tensor(pick[:, :, :], io, top_f[:, :, 0:1].to_broadcast([P, TILES, E]), ALU.is_equal))
            step(nc.vector.tensor_tensor(pick2[:, :, :], io, top_f[:, :, 1:2].to_broadcast([P, TILES, E]), ALU.is_equal))
            step(nc.vector.tensor_tensor(pick[:, :, :], pick[:, :, :], w1[:, :].unsqueeze(2).to_broadcast([P, TILES, E]), ALU.mult))
            step(nc.vector.tensor_tensor(pick2[:, :, :], pick2[:, :, :], w2[:, :].unsqueeze(2).to_broadcast([P, TILES, E]), ALU.mult))
            step(nc.vector.memset(comb[:, :, E:NE], 1.0))
            step(nc.vector.tensor_tensor(comb[:, :, 0:E], pick[:, :, :], pick2[:, :, :], ALU.add))
            step(nc.vector.tensor_copy(comb_hl[:, :, 0:NE], comb[:, :, :]))
            step(nc.vector.tensor_tensor(comb_hl[:, :, NE:2 * NE], comb[:, :, :], comb_hl[:, :, 0:NE].bitcast(F32), ALU.subtract))
            g.comb_steps = n

        @block.tensor
        def _(pe):
            pe.wait_ge(consts_in, 48)
            for b in range(B):
                pe.wait_ge(xn_done, b + 1)
                if b >= 2:
                    pe.wait_ge(lo_done, b - 1)
                for t in range(TPB):
                    ins = nc.tensor.transpose(ps_t[b % 2][:, t * P:(t + 1) * P], x_tok[:, b * TPB + t, :], g.ident[:, :])
                ins.then_inc(xt_ready, 1)
            pe.wait_ge(rw_done, 2)
            for t in range(TILES):
                if t % TPB == 0:
                    pe.wait_ge(lo_done, t // TPB + 1)
                tok = slice(t * P, (t + 1) * P)
                out = ps_lg[:, t * E:(t + 1) * E]
                nc.tensor.matmul(out, g.xh[:, tok], rw_hi[:, :], start=True, stop=False)
                nc.tensor.matmul(out, g.xh[:, tok], rw_lo[:, :], start=False, stop=False)
                ins = nc.tensor.matmul(out, g.xl[:, tok], rw_hi[:, :], start=False, stop=True)
            ins.then_inc(lg_ready, 1)
            pe.wait_ge(comb_done, g.comb_steps)
            for q in range(TILES // 8):
                if q:
                    pe.wait_ge(ct_done, q)
                for t in range(8):
                    ins = nc.tensor.transpose(ps_c[0:2 * NE, t * P:(t + 1) * P],
                                              comb_hl[:, q * 8 + t, :].bitcast(F32), g.ident[:, :])
                ins.then_inc(ct_ready, 1)


def layer0_experts(nc, ctx, g):
    sb, pb, sem = g.scope(ctx)
    KT = NE * FT
    LAG = 3
    NR, NH, NZ = 3, 4, 4
    NW = 2
    up_raw = sb("up_raw", [P, NW, FF], F32)
    dn_raw = sb("dn_raw", [P, NW, FF], F32)
    up_hi = sb("up_hi", [P, NE, FF], F32R)
    up_lo = sb("up_lo", [P, NE, FF], F32R)
    dn_hi = sb("dn_hi", [P, NE, FF], F32R)
    dn_lo = sb("dn_lo", [P, NE, FF], F32R)
    sel_raw = sb("sel_raw", [2 * NE, NE * P], F32)
    sel = sb("sel", [2 * NE, NE * P], F32R)
    r = sb("relu", [P, NR, CH], F32)
    r2 = sb("relu2", [P, NR, CH], F32)
    h_hi = sb("h_hi", [P, NH, CH], F32R)
    h_lo = sb("h_lo", [P, NH, CH], F32R)
    cbs = sb("cbs", [P, 2, CH], F32)
    tmp = sb("moe_tmp", [P, CH], F32)
    acc = sb("moe_acc", [P, CH], F32)
    ps_z = [pb(f"ps_z{i}", [P, CH]) for i in range(NZ)]
    ps_o = [pb(f"ps_o{i}", [P, CH]) for i in range(2)]
    ps_cb = pb("ps_cb", [P, CH])

    w_in = [sem(f"moe_w_in{e}") for e in range(NE)]
    sel_in = sem("sel_in")
    sel_done = sem("sel_done")
    w_hi_done = sem("w_hi_done")
    w_lo_done = sem("w_lo_done")
    z_ready = sem("z_ready")
    relu_done = sem("relu_done")
    sq_done = sem("moe_sq_done")
    hi_done = sem("moe_hi_done")
    lo_done = sem("moe_lo_done")
    down_done = sem("down_done")
    cb_ready = sem("cb_ready")
    cbs_done = sem("cbs_done")
    mix_done = sem("mix_done")
    acc_done = sem("acc_done")
    g_done = sem("g_done")

    with nc.Block() as block:
        @block.sync
        def _(sp):
            sp.dma_start(sel_raw[:, :], g.inp["sel_d"]).then_inc(sel_in, 16)
            for e in range(NE):
                if e >= NW:
                    sp.wait_ge(w_lo_done, 2 * (e - NW) + 2)
                sp.dma_start(up_raw[:, e % NW, :], g.inp["upT"][e]).then_inc(w_in[e], 16)
                sp.dma_start(dn_raw[:, e % NW, :], g.inp["dnT"][e]).then_inc(w_in[e], 16)

        @block.tensor
        def _(pe):
            pe.wait_ge(sel_done, 1)
            with pe.Fori(0, NCH) as c:
                chunk = bass.ds(c * CH, CH)

                def route(e):
                    nc.tensor.matmul(ps_cb[:, :], sel[:, e * P:(e + 1) * P], g.combT[:, chunk],
                                     start=True, stop=True).then_inc(cb_ready, 1)

                def up(k):
                    e, j = divmod(k, FT)
                    pe.wait_ge(w_lo_done, 2 * e + 1)
                    if k >= NZ:
                        pe.wait_ge(relu_done, c * KT + k - NZ + 1)
                    w = slice(j * P, (j + 1) * P)
                    z = ps_z[k % NZ][:, :]
                    nc.tensor.matmul(z, up_hi[:, e, w], g.xh[:, chunk], start=True, stop=False)
                    nc.tensor.matmul(z, up_hi[:, e, w], g.xl[:, chunk], start=False, stop=False)
                    nc.tensor.matmul(z, up_lo[:, e, w], g.xh[:, chunk], start=False, stop=True).then_inc(z_ready, 1)

                def down(k):
                    e, j = divmod(k, FT)
                    if j == 0:
                        pe.wait_ge(w_lo_done, 2 * e + 2)
                        if e >= 2:
                            pe.wait_ge(mix_done, c * NE + e - 1)
                    pe.wait_ge(lo_done, c * KT + k + 1)
                    w = slice(j * P, (j + 1) * P)
                    o = ps_o[e % 2][:, :]
                    nc.tensor.matmul(o, dn_hi[:, e, w], h_hi[:, k % NH, :], start=j == 0, stop=False)
                    nc.tensor.matmul(o, dn_lo[:, e, w], h_hi[:, k % NH, :], start=False, stop=False)
                    nc.tensor.matmul(o, dn_hi[:, e, w], h_lo[:, k % NH, :], start=False,
                                     stop=j == FT - 1).then_inc(down_done, 1)

                for k in range(KT + LAG):
                    if k < KT:
                        if k and k % FT == 0:
                            pe.wait_ge(cbs_done, c * NE + k // FT)
                        up(k)
                        if k % FT == 0:
                            route(k // FT)
                    if k >= LAG:
                        down(k - LAG)

        @block.scalar
        def _(act):
            act.wait_ge(sel_in, 16)
            nc.scalar.activation(sel[:, :], sel_raw[:, :], ACT.Copy).then_inc(sel_done, 1)
            for e in range(NE):
                act.wait_ge(w_in[e], 32)
                nc.scalar.activation(up_hi[:, e, :], up_raw[:, e % NW, :], ACT.Copy).then_inc(w_hi_done, 1)
                nc.scalar.activation(dn_hi[:, e, :], dn_raw[:, e % NW, :], ACT.Copy).then_inc(w_hi_done, 1)
            with act.Fori(0, NCH) as c:
                def high(k):
                    act.wait_ge(sq_done, c * KT + k + 1)
                    if k >= NH:
                        act.wait_ge(down_done, c * KT + k - NH + 1)
                    nc.scalar.activation(h_hi[:, k % NH, :], r2[:, k % NR, :], ACT.Copy).then_inc(hi_done, 1)

                for k in range(KT + 1):
                    if k < KT:
                        act.wait_ge(z_ready, c * KT + k + 1)
                        if k >= NR:
                            act.wait_ge(sq_done, c * KT + k - NR + 1)
                        nc.scalar.activation(r[:, k % NR, :], ps_z[k % NZ][:, :], ACT.Relu).then_inc(relu_done, 1)
                        if k % FT == 2:
                            e = k // FT
                            act.wait_ge(cb_ready, c * NE + e + 1)
                            if e >= 2:
                                act.wait_ge(mix_done, c * NE + e - 1)
                            nc.scalar.activation(cbs[:, e % 2, :], ps_cb[:, :], ACT.Copy).then_inc(cbs_done, 1)
                    if k >= 1:
                        high(k - 1)
                act.wait_ge(acc_done, (c + 1) * NE)
                nc.scalar.activation(g.gT[:, bass.ds(c * CH, CH)], acc[:, :], ACT.Silu).then_inc(g_done, 1)

        @block.gpsimd
        def _(pool):
            with pool.Fori(0, NCH) as c:
                for k in range(KT):
                    pool.wait_ge(relu_done, c * KT + k + 1)
                    if k >= NR:
                        pool.wait_ge(lo_done, c * KT + k - NR + 1)
                    nc.gpsimd.tensor_tensor(r2[:, k % NR, :], r[:, k % NR, :], r[:, k % NR, :],
                                            ALU.mult).then_inc(sq_done, 1)

        @block.vector
        def _(v):
            for e in range(NE):
                v.wait_ge(w_hi_done, 2 * e + 1)
                nc.vector.tensor_tensor(up_lo[:, e, :], up_raw[:, e % NW, :], up_hi[:, e, :].bitcast(F32),
                                        ALU.subtract).then_inc(w_lo_done, 1)
                v.wait_ge(w_hi_done, 2 * e + 2)
                nc.vector.tensor_tensor(dn_lo[:, e, :], dn_raw[:, e % NW, :], dn_hi[:, e, :].bitcast(F32),
                                        ALU.subtract).then_inc(w_lo_done, 1)
            nc.vector.memset(tmp[:, 0:1], 0.0).then_inc(g_done, 1)
            with v.Fori(0, NCH) as c:
                def mix(e):
                    v.wait_ge(down_done, c * KT + (e + 1) * FT)
                    v.wait_ge(cbs_done, c * NE + e + 1)
                    if e == 0:
                        v.wait_ge(g_done, c + 1)
                        nc.vector.tensor_tensor(acc[:, :], ps_o[0][:, :], cbs[:, 0, :], ALU.mult).then_inc(mix_done, 1)
                        v.wait_ge(mix_done, c * NE + 1)
                        v.sem_inc(acc_done, 1)
                    else:
                        if e >= 2:
                            v.wait_ge(acc_done, c * NE + e)
                        nc.vector.tensor_tensor(tmp[:, :], ps_o[e % 2][:, :], cbs[:, e % 2, :],
                                                ALU.mult).then_inc(mix_done, 1)
                        v.wait_ge(mix_done, c * NE + e + 1)
                        nc.vector.tensor_tensor(acc[:, :], acc[:, :], tmp[:, :], ALU.add).then_inc(acc_done, 1)

                for k in range(KT + 1):
                    if k < KT:
                        v.wait_ge(hi_done, c * KT + k + 1)
                        nc.vector.tensor_tensor(h_lo[:, k % NH, :], r2[:, k % NR, :], h_hi[:, k % NH, :].bitcast(F32),
                                                ALU.subtract).then_inc(lo_done, 1)
                    e = (k - FT - LAG) // FT
                    if k >= FT + LAG and (k - FT - LAG) % FT == 1:
                        mix(e)
                mix(NE - 1)


def layer0_attention(nc, ctx, g):
    sb, pb, sem = g.scope(ctx)
    N = B * PAIRS
    KT = T // P
    STEPS = 2 * KT
    CK = 2 * STEPS
    SCALE = DH ** -0.5
    NM = 8
    K2R = DH + NM
    NPR = 8
    HALVES = 16
    HALF_AT = [3, 3, 3, 1, 3, 3, 0, 0]
    ADDS = 2 * (KT - 2)
    ADD0 = 6

    qkv = sb("qkv_raw", [P, PAIRS, 3, 2 * DH], F32)
    wout = sb("wout_raw", [P, PAIRS, D], F32)
    w_hi = sb("w_hi", [P, 3, 2 * DH], F32R)
    w_lo = sb("w_lo", [P, 3, 2 * DH], F32R)
    wo = [sb(f"wo{i}", [P, D], F32) for i in range(2)]
    Q1 = [[sb(f"Q1_{p}{x}", [P, T], F32R) for x in range(2)] for p in range(2)]
    Q2 = [[sb(f"Q2_{p}{x}", [K2R, T], F32R) for x in range(2)] for p in range(2)]
    K1 = [[sb(f"K1_{p}{x}", [P, T], F32R) for x in range(2)] for p in range(2)]
    K2 = [[sb(f"K2_{p}{x}", [K2R, T], F32R) for x in range(2)] for p in range(2)]
    vT = sb("vT", [P, T], F32)
    V = [sb(f"V{p}", [P, KT, 2 * DH], F32) for p in range(2)]
    probs = sb("probs", [P, NPR, CH], F32)
    psum_k = [[sb(f"psum_k{h}{x}", [P, CH], F32) for x in range(2)] for h in range(2)]
    rden = sb("rden", [P, CH], F32)
    attn = sb("attn", [P, CH], F32)
    mxh = sb("mxh", [P, NM, 2], F32)
    mx = sb("mx", [P, NM], F32)
    mT = sb("mT", [K2R, P], F32)
    mask = sb("mask", [K2R, 2, CH], F32)
    ones = sb("ones", [P, DH], F32)
    ps_s = [pb(f"ps_s{i}", [P, CH]) for i in range(2)]
    ps_m = [pb(f"ps_m{i}", [P, CH]) for i in range(2)]
    ps_v = [pb(f"ps_v{i}", [P, CH]) for i in range(2)]
    ps_x = [pb(f"ps_x{i}", [P, CH]) for i in range(2)]

    w_in = sem("attn_w_in")
    preset = sem("preset")
    w_staged = sem("w_staged")
    wlo_staged = sem("wlo_staged")
    s_ready = sem("s_ready")
    p_done = sem("p_done")
    pv_done = sem("pv_done")
    add_done = sem("add_done")
    m_ready = sem("m_ready")
    m_done = sem("m_done")
    mx_done = sem("mx_done")
    q2_done = sem("q2_done")
    x_ready = sem("x_ready")
    hi_done = sem("qk_hi_done")
    xa_done = sem("xa_done")
    xv_done = sem("xv_done")
    rden_done = sem("rden_done")
    attn_done = sem("attn_done")

    LIST = [("K0", 0, "v"), ("K1", 1, "v"), ("den1", 2, "v"), ("Q0", 3, "v"), ("out1", 4, "v"), ("Q1", 5, "v"),
            ("max1", 6, "a"), ("V0", 7, "a"), ("V1", 8, "a"), ("VT0", 9, "a"), ("den0", 10, "v"), ("VT1", 11, "a"),
            ("out0", 12, "v"), ("max0", 14, "a")]
    FIRST = ["K0", "K1", "Q0", "Q1", "V0", "V1", "VT0", "VT1", "max0"]
    LAST = ["den1", "out1"]
    PLACE = {name: i for i, (name, _, _) in enumerate(LIST)}
    STEP = {step: name for name, step, _ in LIST}
    READER = {name: r for name, _, r in LIST}
    PER = {c: sum(r == c for r in READER.values()) for c in "av"}
    AHEAD = {c: sum(READER[n] == c for n in FIRST) for c in "av"}
    READ = {"a": xa_done, "v": xv_done}

    def nth(n, name):
        if n is N:
            return N * len(LIST) + len(FIRST) + LAST.index(name) + 1
        return FIRST.index(name) + 1 if n is None else n * len(LIST) + len(FIRST) + PLACE[name] + 1

    def reads(n, name):
        c = READER[name]
        if n is None:
            return sum(READER[k] == c for k in FIRST[:FIRST.index(name) + 1])
        if n is N:
            return N * PER[c] + AHEAD[c] + LAST.index(name) + 1
        return n * PER[c] + AHEAD[c] + sum(r == c for _, _, r in LIST[:PLACE[name] + 1])

    def rounded(n, name):
        names = FIRST if n is None else [k for k, _, _ in LIST]
        upto = sum(k[0] in "KQ" for k in names[:names.index(name) + 1])
        return upto if n is None else n * 4 + 4 + upto

    def bank(n, name):
        u = FIRST.index(name) + 1 if n is None else len(FIRST) + 1 + PLACE[name]
        return ps_x[u % 2]

    def added(t):
        hf, kt = divmod(t, KT)
        return hf * ADDS + 2 * min(max(kt, 1), KT - 2)

    def half_rows(t):
        at = t % KT
        first = sum(HALF_AT[:at])
        return range(first, first + HALF_AT[at])

    def pairs(eng):
        with eng.Fori(0, N // 2) as i:
            for par in range(2):
                yield i * 2 + par, par

    with nc.Block() as block:
        @block.sync
        def _(sp):
            sp.dma_start(qkv[:, :, :, :], g.inp["qkv_d"]).then_inc(w_in, 16)
            sp.dma_start(wout[:, :, :], g.inp["wout_d"]).then_inc(w_in, 16)
            sp.dma_start(mask[DH:K2R, :, :], g.inp["mask_d"]).then_inc(w_in, 16)

        @block.tensor
        def _(pe):
            def other(n, par, name, b):
                o = bank(n, name)
                if n is None:
                    i = FIRST.index(name)
                    if i >= 2:
                        pe.wait_ge(READ[READER[FIRST[i - 2]]], reads(n, FIRST[i - 2]))
                elif n is N:
                    pe.wait_ge(xa_done, N * PER["a"] + AHEAD["a"])
                    pe.wait_ge(xv_done, N * PER["v"] + AHEAD["v"])
                elif PLACE[name] >= 2:
                    before = LIST[PLACE[name] - 2][0]
                    pe.wait_ge(READ[READER[before]], reads(n, before))
                else:
                    pe.wait_ge(xv_done, n * PER["v"] + AHEAD["v"])
                    pe.wait_ge(xa_done, n * PER["a"] + AHEAD["a"] - 1 + PLACE[name])
                if name[0] in "KQ" or name in ("V0", "V1"):
                    c = "QKV".index(name[0])
                    tok = bass.ds(b * T + int(name[1]) * CH, CH)
                    if name == "K0":
                        pe.wait_ge(w_staged, 1 if n is None else n + 2)
                        pe.wait_ge(wlo_staged, 1 if n is None else n + 2)
                    nc.tensor.matmul(o[:, :], w_hi[:, c, :], g.xh[:, tok], start=True, stop=False)
                    nc.tensor.matmul(o[:, :], w_hi[:, c, :], g.xl[:, tok], start=False, stop=False)
                    ins = nc.tensor.matmul(o[:, :], w_lo[:, c, :], g.xh[:, tok], start=False, stop=True)
                elif name in ("VT0", "VT1"):
                    pe.wait_ge(xa_done, reads(n, "V" + name[2]))
                    for t in range(CH // P):
                        col = int(name[2]) * CH + t * P
                        ins = nc.tensor.transpose(o[:, t * P:(t + 1) * P], vT[:, col:col + P], g.ident[:, :])
                elif name in ("max0", "max1"):
                    unit = 0 if n is None else n * 2 + (1 if name == "max1" else 2)
                    pe.wait_ge(mx_done, unit + 1)
                    ins = nc.tensor.matmul(o[DH:K2R, 0:P], mx[:, :], g.ident[:, :], start=True, stop=True)
                elif name in ("den0", "den1"):
                    hf = int(name[3])
                    pe.wait_ge(add_done, ADD0 + n * 2 * ADDS + (0 if hf else ADDS))
                    for x in range(2):
                        rows = slice(x * DH, (x + 1) * DH)
                        last = (2 * (KT * hf + KT - 1) + x) % NPR
                        nc.tensor.matmul(o[rows, :], ones[:, :], psum_k[hf][x][:, :], start=True, stop=False)
                        ins = nc.tensor.matmul(o[rows, :], ones[:, :], probs[:, last, :], start=False, stop=True)
                else:
                    hf = int(name[3])
                    pe.wait_ge(attn_done, n * 2 + (1 if hf else 2))
                    ins = nc.tensor.matmul(o[:, :], wo[1 - par if hf else par][:, :], attn[:, :], start=True, stop=True)
                ins.then_inc(x_ready, 1)

            def half_row(unit, i, par, hf):
                x, t, kh = i // 8, i // 2 % 4, i % 2
                if unit is None:
                    if i >= 2:
                        pe.wait_ge(m_done, i - 1)
                else:
                    pe.wait_ge(m_done, unit * HALVES + i - 1)
                q = hf * CH + t * P
                nc.tensor.matmul(ps_m[i % 2][:, :], Q1[par][x][:, q:q + P], K1[par][x][:, kh * CH:(kh + 1) * CH],
                                 start=True, stop=True).then_inc(m_ready, 1)

            def values(n, par, t):
                hf, kt = divmod(t, KT)
                for x in range(2):
                    k = 2 * t + x
                    pe.wait_ge(p_done, n * CK + k + 1)
                    rows = slice(x * DH, (x + 1) * DH)
                    nc.tensor.matmul(ps_v[hf][rows, :], V[par][:, kt, rows], probs[:, k % NPR, :],
                                     start=kt == 0, stop=kt == KT - 1).then_inc(pv_done, 1)

            pe.wait_ge(preset, 3)
            for name in FIRST:
                if name == "max0":
                    pe.wait_ge(xv_done, reads(None, "Q1"))
                    for i in range(HALVES):
                        half_row(None, i, 0, 0)
                other(None, 0, name, 0)
            for x in range(2):
                nc.tensor.matmul(ps_v[1][x * DH:(x + 1) * DH, :], ones[:, :], probs[:, x, :], start=True, stop=True)
            for n, par in pairs(pe):
                b = (n + 1) // PAIRS % B
                for t in range(STEPS):
                    hf, kt = divmod(t, KT)
                    keys, qs = slice(kt * P, (kt + 1) * P), slice(hf * CH, (hf + 1) * CH)
                    if kt == 0:
                        pe.wait_ge(q2_done, n * 4 + 2 * hf + 2)
                    for x in range(2):
                        if t:
                            pe.wait_ge(p_done, n * CK + 2 * t + x - 1)
                        nc.tensor.matmul(ps_s[x][:, :], K1[par][x][:, keys], Q1[par][x][:, qs], start=True, stop=False)
                        nc.tensor.matmul(ps_s[x][:, :], K2[par][x][:, keys], Q2[par][x][:, qs],
                                         start=False, stop=True).then_inc(s_ready, 1)
                    if t in STEP:
                        other(n, par, STEP[t], b)
                    if t == KT:
                        pe.wait_ge(xv_done, reads(n, "Q1"))
                    for i in half_rows(t):
                        half_row(n * 2 + 1 + hf, i, par if hf == 0 else 1 - par, 1 - hf)
                    if t >= 2:
                        values(n, par, t - 2)
                values(n, par, STEPS - 2)
                values(n, par, STEPS - 1)
            for name in LAST:
                other(N, 0, name, 0)

        @block.scalar
        def _(act):
            def stage(n, par):
                nc.scalar.activation(wo[1 - par][:, :], wout[:, bass.ds((n + 1) % PAIRS, 1), :].rearrange("p a d -> p (a d)"), ACT.Copy)
                nc.scalar.activation(w_hi[:, :, :].rearrange("p c d -> p (c d)"),
                                     qkv[:, bass.ds((n + 2) % PAIRS, 1), :, :].rearrange("p a c d -> p (a c d)"),
                                     ACT.Copy).then_inc(w_staged, 1)

            def read(n, name, par):
                if READER[name] == "v" and name[0] not in "KQ":
                    return
                o = bank(n, name)
                act.wait_ge(x_ready, nth(n, name))
                if name[0] in "KQ":
                    cols = slice(int(name[1]) * CH, (int(name[1]) + 1) * CH)
                    for x in range(2):
                        rows = o[x * DH:(x + 1) * DH, :]
                        if name[0] == "K":
                            nc.scalar.activation(K1[par][x][0:DH, cols], rows, ACT.Copy)
                            ins = nc.scalar.activation(K1[par][x][DH:P, cols], rows, ACT.Copy)
                        else:
                            nc.scalar.activation(Q1[par][x][0:DH, cols], rows, ACT.Copy)
                            ins = nc.scalar.activation(Q2[par][x][0:DH, cols], rows, ACT.Copy)
                    ins.then_inc(hi_done, 1)
                elif name in ("V0", "V1"):
                    cols = slice(int(name[1]) * CH, (int(name[1]) + 1) * CH)
                    nc.scalar.activation(vT[:, cols], o[:, :], ACT.Copy).then_inc(xa_done, 1)
                elif name in ("VT0", "VT1"):
                    half = int(name[2])
                    tiles = V[par][:, 4 * half:4 * half + 4, :].rearrange("p t d -> p (t d)")
                    nc.scalar.activation(tiles, o[:, :], ACT.Copy).then_inc(xa_done, 1)
                else:
                    if n is not None:
                        act.wait_ge(q2_done, n * 4 + (2 if name == "max1" else 4))
                    nc.scalar.activation(mT[DH:K2R, :], o[DH:K2R, 0:P], ACT.Copy).then_inc(xa_done, 1)

            act.wait_ge(w_in, 48)
            nc.scalar.activation(wo[0][:, :], wout[:, 0, :], ACT.Copy)
            nc.scalar.activation(wo[1][:, :], wout[:, 1, :], ACT.Copy)
            nc.scalar.activation(w_hi[:, :, :], qkv[:, 0, :, :], ACT.Copy).then_inc(w_staged, 1)
            for name in FIRST:
                read(None, name, 0)
                if name == "V1":
                    nc.scalar.activation(w_hi[:, :, :], qkv[:, 1, :, :], ACT.Copy).then_inc(w_staged, 1)
            for n, par in pairs(act):
                for t in range(STEPS):
                    for x in range(2):
                        k = 2 * t + x
                        act.wait_ge(s_ready, n * CK + k + 1)
                        if x == 0:
                            if t >= 4:
                                act.wait_ge(add_done, ADD0 + n * 2 * ADDS + added(t - 4))
                                act.wait_ge(pv_done, n * CK + 2 * (t - 4) + 2)
                            else:
                                act.wait_ge(add_done, ADD0 + n * 2 * ADDS + added(t + STEPS - 4) - 2 * ADDS)
                            if t in (3, KT + 3):
                                act.wait_ge(x_ready, nth(n, "den1" if t == 3 else "den0"))
                        nc.scalar.activation(probs[:, k % NPR, :], ps_s[x][:, :], ACT.Exp, scale=SCALE).then_inc(p_done, 1)
                    if t in STEP:
                        name = STEP[t]
                        read(n, name, 1 - par)
                    if t == 12:
                        stage(n, par)

        @block.gpsimd
        def _(pool):
            def rest(src):
                nc.gpsimd.tensor_tensor(w_lo[:, :, :].rearrange("p c d -> p (c d)"), src,
                                        w_hi[:, :, :].rearrange("p c d -> p (c d)").bitcast(F32),
                                        ALU.subtract).then_inc(wlo_staged, 1)

            def spread(n, name, par, hf):
                pool.wait_ge(xa_done, reads(n, name))
                if n is None:
                    pool.wait_ge(wlo_staged, 2)
                else:
                    pool.wait_ge(add_done, ADD0 + n * 2 * ADDS + (2 if name == "max0" else 1) * ADDS)
                for x in range(2):
                    nc.gpsimd.tensor_tensor(
                        Q2[par][x][DH:K2R, hf * CH:(hf + 1) * CH].rearrange("p (j q) -> p j q", j=4),
                        mT[DH:K2R, :].unsqueeze(1).to_broadcast([NM, 4, P]),
                        mask[DH:K2R, x, :].rearrange("p (j q) -> p j q", j=4), ALU.mult).then_inc(q2_done, 1)
                pool.wait_ge(q2_done, 2 if n is None else n * 4 + (6 if name == "max0" else 4))

            nc.gpsimd.memset(probs[:, :, :], 0.0).then_inc(preset, 1)
            nc.gpsimd.memset(ones[:, :], 1.0).then_inc(preset, 1)
            for x in range(2):
                nc.gpsimd.memset(psum_k[1][x][:, :], 1.0).then_inc(add_done, 1)
            pool.wait_ge(w_staged, 1)
            rest(qkv[:, 0, :, :].rearrange("p c d -> p (c d)"))
            pool.wait_ge(w_staged, 2)
            rest(qkv[:, 1, :, :].rearrange("p c d -> p (c d)"))
            spread(None, "max0", 0, 0)
            for n, par in pairs(pool):
                for t in range(STEPS):
                    hf, kt = divmod(t, KT)
                    if 1 <= kt <= KT - 2:
                        for x in range(2):
                            k = 2 * t + x
                            pool.wait_ge(p_done, n * CK + k + 1)
                            if kt > 1:
                                pool.wait_ge(add_done, ADD0 + n * 2 * ADDS + hf * ADDS + 2 * (kt - 2) + x + 1)
                            acc = psum_k[hf][x][:, :]
                            nc.gpsimd.tensor_tensor(acc, probs[:, (k - 2) % NPR, :] if kt == 1 else acc,
                                                    probs[:, k % NPR, :], ALU.add).then_inc(add_done, 1)
                    if t == 6:
                        spread(n, "max1", par, 1)
                    if t == 12:
                        pool.wait_ge(w_staged, n + 3)
                        rest(qkv[:, bass.ds((n + 2) % PAIRS, 1), :, :].rearrange("p a c d -> p (a c d)"))
                    if t == 14:
                        pool.wait_ge(wlo_staged, n + 3)
                        spread(n, "max0", 1 - par, 0)

        @block.vector
        def _(v):
            def half_max(unit, i):
                v.wait_ge(m_ready, i + 1 if unit is None else unit * HALVES + i + 1)
                nc.vector.tensor_reduce(mxh[:, i // 2, i % 2:i % 2 + 1], ps_m[i % 2][:, :], AX.X, ALU.max).then_inc(m_done, 1)
                if i == HALVES - 1:
                    v.wait_ge(m_done, HALVES if unit is None else unit * HALVES + HALVES)
                    nc.vector.tensor_reduce(mx[:, :], mxh[:, :, :], AX.X, ALU.max).then_inc(mx_done, 1)

            def read(n, name, par):
                if READER[name] != "v":
                    return
                o = bank(n, name)
                if name[0] in "KQ":
                    v.wait_ge(hi_done, rounded(n, name))
                    cols = slice(int(name[1]) * CH, (int(name[1]) + 1) * CH)
                    for x in range(2):
                        hi = K1 if name[0] == "K" else Q1
                        low = K2[par][x][0:DH, cols] if name[0] == "K" else Q1[par][x][DH:P, cols]
                        ins = nc.vector.tensor_tensor(low, o[x * DH:(x + 1) * DH, :], hi[par][x][0:DH, cols].bitcast(F32), ALU.subtract)
                    ins.then_inc(xv_done, 1)
                elif name[:3] == "den":
                    hf = int(name[3])
                    v.wait_ge(x_ready, nth(n, name))
                    nc.vector.reciprocal(rden[:, :], o[:, :]).then_inc(xv_done, 1)
                    v.wait_ge(xv_done, reads(n, name))
                    if hf == 0:
                        v.wait_ge(pv_done, n * CK + CK // 2)
                    nc.vector.tensor_tensor(attn[:, :], ps_v[hf][:, :], rden[:, :], ALU.mult).then_inc(attn_done, 1)
                else:
                    unit = n * 2 + (B * PAIRS * 2 - 1 if name == "out1" else 0)
                    v.wait_ge(x_ready, nth(n, name))
                    pair = unit // 2 % N
                    tok = bass.ds(pair // PAIRS * T + int(name[3]) * CH, CH)
                    nc.vector.tensor_tensor(g.sT[:, tok], o[:, :], g.sT[:, tok], ALU.add).then_inc(xv_done, 1)

            nc.vector.memset(g.sT[:, :], 0.0).then_inc(preset, 1)
            for p in range(2):
                for x in range(2):
                    nc.vector.memset(K2[p][x][DH:K2R, :].bitcast(F32), 1.0).then_inc(add_done, 1)
            for name in FIRST:
                if name == "max0":
                    for i in range(HALVES):
                        half_max(None, i)
                read(None, name, 0)
            for n, par in pairs(v):
                for t in range(STEPS):
                    for i in half_rows(t):
                        half_max(n * 2 + 1 + t // KT, i)
                    if t in STEP:
                        read(n, STEP[t], 1 - par)
            for name in LAST:
                read(N, name, 0)


def fp4(nc, step, x, s, rs, v, av, hi, low, out):
    p, nb, _ = x.shape

    def ints(a):
        return a.bitcast(U32)

    def over(m, acc):
        step(nc.vector.scalar_tensor_tensor(acc, av, m, acc, ALU.is_gt, ALU.add))

    step(nc.vector.tensor_reduce(s, x, AX.X, ALU.max, apply_absolute_value=True))
    step(nc.vector.tensor_scalar(s, s, 1.0 / 6.0, 1e-12, ALU.mult, ALU.max))
    step(nc.vector.reciprocal(rs, s))
    step(nc.vector.tensor_tensor(v, x, rs.unsqueeze(2).to_broadcast([p, nb, BLK]), ALU.mult))
    step(nc.vector.tensor_scalar(ints(av), ints(v), 0x7FFFFFFF, None, ALU.bitwise_and))
    step(nc.vector.tensor_scalar(hi, av, 5.0, 2.0, ALU.is_gt, ALU.mult))
    over(3.5, hi)
    over(2.5, hi)
    step(nc.vector.tensor_scalar(low, av, 1.75, 1.0, ALU.is_gt, ALU.mult))
    over(1.25, low)
    over(0.75, low)
    over(0.25, low)
    step(nc.vector.scalar_tensor_tensor(hi, low, 0.5, hi, ALU.mult, ALU.add))
    step(nc.vector.scalar_tensor_tensor(ints(hi), ints(v), 0x80000000, ints(hi), ALU.bitwise_and, ALU.bitwise_or))
    step(nc.vector.tensor_tensor(out, hi, s.unsqueeze(2).to_broadcast([p, nb, BLK]), ALU.mult))


FP4_STEPS = 15


def layer1(nc, ctx, g):
    sb, pb, sem = g.scope(ctx)
    TC = CH // P
    NB = TC * D // BLK
    NBI = INNER // BLK
    HALF = T // CH

    x1 = sb("x1", [P, TILES, D], F32)
    xn = sb("xn2", [P, TILES, D], F32)
    sq = sb("sq2", [P, TPB, D], F32)
    u = sb("u_tok", [P, TPB, D], F32)
    sums = sb("sums2", [P, TPB], F32)
    neg_mean = sb("neg_mean2", [P, TPB], F32)
    var = sb("var2", [P, 2, TPB], F32)
    rstd = sb("rstd2", [P, 2, TPB], F32)
    mhalf = sb("mhalf2", [P, TPB], F32)
    uT = sb("uT", [P, T], F32)
    ud = sb("ud", [P, 2, T], F32)
    states = sb("states", [P, 2, T], F32)
    bmat = sb("bmat", [P, S], F32)
    cmat = sb("cmat", [P, D], F32)
    dcol = sb("dcol", [P, 1], F32)
    nw = sb("nw", [P, 1], F32)
    dt = sb("dt", [P, 1], F32)
    acol = sb("acol", [P, 1], F32)
    et = sb("et", [P, 1], F32)
    dts = sb("dts", [P, 1], F32)
    decay = sb("decay", [P, 1], F32)
    w_gu = sb("w_gu", [P, 6, D], F32)
    w_dn = sb("w_dn", [P, INNER], F32)
    wq_gu = sb("wq_gu", [P, 6, D], F32)
    wq_dn = sb("wq_dn", [P, INNER], F32)
    wT_gu = sb("wT_gu", [P, 2 * INNER], F32)
    wT_dn = sb("wT_dn", [P, 3, D], F32)
    NBMAX = TC * NBI
    s_ = sb("q_s", [P, NBMAX], F32)
    rs_ = sb("q_rs", [P, NBMAX], F32)
    v_ = sb("q_v", [P, NBMAX, BLK], F32)
    av_ = sb("q_av", [P, NBMAX, BLK], F32)
    hi_ = sb("q_hi", [P, NBMAX, BLK], F32)
    low_ = sb("q_low", [P, NBMAX, BLK], F32)
    xq = sb("xq", [P, TC, D], F32)
    xqT = sb("xqT", [P, CH], F32)
    sg = sb("sg", [P, 2, INNER], F32)
    h = sb("h", [P, TC, INNER], F32)
    hqT = sb("hqT", [P, 3, CH], F32)
    g1 = sb("g1", [P, CH], F32)
    pr2 = sb("pr2", [P, CH], F32)
    out_t = sb("out_t", [P, TC, D], F32)
    ps_a = pb("ps_a", [P, T])
    ps_b = pb("ps_b", [P, T])
    ps_c = pb("ps_c1", [P, T])
    ps_d = [pb(f"ps_d{i}", [P, CH]) for i in range(2)]

    x_in = [sem(f"x1_in{b}") for b in range(B)]
    c_in = sem("l1_consts_in")
    w_in = sem("l1_weights_in")
    w_zero = sem("l1_w_zero")
    pr_done = sem("pr_done")
    mh = sem("mh2")
    prT_ready = sem("prT_ready")
    chain = sem("l1_chain")
    c_step = sem("l1_c_step")
    mid_done = sem("mid_done")
    sq_done = sem("sq2_done")
    var_done = sem("var2_done")
    rstd_done = sem("rstd2_done")
    u_done = sem("u_done")
    uT_ready = sem("uT_ready")
    uT_done = sem("uT_done")
    up_ready = sem("up_ready")
    ud_done = sem("ud_done")
    scan_done = sem("scan_done")
    y_ready = sem("y_ready")
    y_done = sem("y_done")
    et_done = sem("et_done")
    dts_done = sem("dts_done")
    a_done = sem("a_done")
    wq_done = sem("wq_done")
    wT_ready = sem("wT_ready")
    wT_done = sem("wT_done")
    xq_done = sem("xq_done")
    xqT_ready = sem("xqT_ready")
    xqT_done = sem("xqT_done")
    gu_ready = sem("gu_ready")
    sg_done = sem("sg_done")
    h_done = sem("h_done")
    hq_done = sem("hq_done")
    hT_ready = sem("hT_ready")
    hT_done = sem("hT_done")
    dn_ready = sem("dn_ready")
    g1_done = sem("g1_done")
    pr2_done = sem("pr2_done")
    o_ready = sem("o_ready")
    o_done = sem("o_done")
    stored = sem("stored")

    def rows(b):
        return slice(b * TPB, (b + 1) * TPB)

    with nc.Block() as block:
        @block.sync
        def _(sp):
            for b in range(B):
                sp.dma_start(x1[:, rows(b), :], g.inp["X"][b].rearrange("(n p) d -> p n d", p=P)).then_inc(x_in[b], 16)
            for dst, src in ((bmat, g.inp["Bmat_d"]), (cmat, g.inp["C_d"]), (dcol, g.inp["D_d"]), (nw, g.inp["norm_w_d"]), (dt, g.inp["dt_d"]), (acol, g.inp["A_d"])):
                sp.dma_start(dst[:, :], src).then_inc(c_in, 16)
            sp.wait_ge(w_zero, 1)
            for k, w in enumerate((g.inp["w_gate_d"], g.inp["w_up_d"])):
                for j, (lo, n) in enumerate(IB):
                    sp.dma_start(w_gu[0:n, 3 * k + j, :], w[lo:lo + n, :]).then_inc(w_in, 16)
            sp.dma_start(w_dn[:, :], g.inp["w_down_d"]).then_inc(w_in, 16)
            with sp.Fori(0, NCH) as c:
                sp.wait_ge(o_done, c + 1)
                dst = g.out[bass.ds(c // HALF, 1), bass.ds(c % HALF * CH, CH), :].rearrange("a (n p) d -> p (a n) d", p=P)
                sp.dma_start(dst, out_t[:, :, :]).then_inc(stored, 16)
            sp.wait_ge(stored, 16 * NCH + 1)

        @block.gpsimd
        def _(pool):
            nc.gpsimd.memset(mhalf[:, :], -0.5).then_inc(mh, 1)
            nc.gpsimd.memset(w_gu[:, :, :], 0.0).then_inc(w_zero, 1)
            for b in range(B):
                tok = slice(b * T, (b + 1) * T)
                nc.gpsimd.tensor_tensor(g.sT[:, tok], g.sT[:, tok], g.gT[:, tok], ALU.mult).then_inc(pr_done, 1)
            pool.wait_ge(mh, 1)
            for b in range(B):
                for k in range(2):
                    pool.wait_ge(var_done, 2 * b + k + 1)
                    nc.gpsimd.tensor_tensor(rstd[:, k, :], var[:, k, :], mhalf[:, :], ALU.pow).then_inc(rstd_done, 1)
            with pool.Fori(0, NCH) as c:
                tok = bass.ds(c * CH, CH)
                pool.wait_ge(y_done, B * HALF)
                pool.wait_ge(g1_done, c + 1)
                nc.gpsimd.tensor_tensor(pr2[:, :], g.sT[:, tok], g1[:, :], ALU.mult).then_inc(pr2_done, 1)

        @block.scalar
        def _(act):
            act.wait_ge(c_in, 6 * 16)
            nc.scalar.activation(et[:, :], dt[:, :], ACT.Exp, scale=-1.0).then_inc(et_done, 1)
            act.wait_ge(dts_done, 1)
            nc.scalar.activation(decay[:, :], decay[:, :], ACT.Exp).then_inc(a_done, 1)
            for b in range(B):
                for k in range(2):
                    act.wait_ge(mid_done, 2 * b + k + 1)
                    nc.scalar.activation(sq[:, :, :], xn[:, rows(b), :], ACT.Square).then_inc(sq_done, 1)
                act.wait_ge(uT_ready, b + 1)
                if b:
                    act.wait_ge(up_ready, b)
                nc.scalar.activation(uT[:, :], ps_b[:, :], ACT.Copy, scale=nw[:, 0:1]).then_inc(uT_done, 1)
                act.wait_ge(up_ready, b + 1)
                r = slice(b % 2 * S, (b % 2 + 1) * S)
                nc.scalar.activation(ud[r, b // 2, :], ps_c[r, :], ACT.Copy, scale=dts[r, 0:1]).then_inc(ud_done, 1)
            for q in range(B):
                act.wait_ge(y_ready, q + 1)
                act.wait_ge(prT_ready, B)
                tok = slice(q * T, (q + 1) * T)
                nc.scalar.activation(g.sT[:, tok], (ps_a, ps_b)[q % 2][:, :], ACT.Identity, bias=dcol[:, 0:1]).then_inc(y_done, 2)
            act.wait_ge(wT_ready, 1)
            for k in range(2):
                nc.scalar.activation(wT_gu[:, k * INNER:(k + 1) * INNER], ps_d[k][:, 0:INNER], ACT.Copy)
            for j, (lo, n) in enumerate(IB):
                ins = nc.scalar.activation(wT_dn[0:n, j, :], ps_a[0:n, j * P:(j + 1) * P], ACT.Copy)
            ins.then_inc(wT_done, 1)
            with act.Fori(0, NCH) as c:
                act.wait_ge(xqT_ready, c + 1)
                nc.scalar.activation(xqT[:, :], ps_a[:, 0:CH], ACT.Copy).then_inc(xqT_done, 1)
                for t in range(TC):
                    act.wait_ge(gu_ready, c * TC + t + 1)
                    if t >= 2:
                        act.wait_ge(h_done, c * TC + t - 1)
                    nc.scalar.activation(sg[:, t % 2, :], ps_d[t % 2][:, 0:INNER], ACT.Silu).then_inc(sg_done, 1)
                act.wait_ge(hT_ready, c + 1)
                for j, (lo, n) in enumerate(IB):
                    src = (ps_b[0:n, 0:CH], ps_b[0:n, CH:T], ps_a[0:n, CH:T])[j]
                    ins = nc.scalar.activation(hqT[0:n, j, :], src, ACT.Copy)
                ins.then_inc(hT_done, 1)
                act.wait_ge(dn_ready, c + 1)
                nc.scalar.activation(g1[:, :], ps_a[:, 0:CH], ACT.Silu).then_inc(g1_done, 1)

        @block.vector
        def _(v):
            n = 0

            def step(ins):
                nonlocal n
                n += 1
                ins.then_inc(chain, 1)
                v.wait_ge(chain, n)

            v.sem_inc(stored, 1)
            v.wait_ge(et_done, 1)
            step(nc.vector.tensor_scalar(et[:, :], et[:, :], 1.0, None, ALU.add))
            step(nc.vector.reciprocal(dts[:, :], et[:, :]))
            step(nc.vector.tensor_scalar(acol[:, :].bitcast(U32), acol[:, :].bitcast(U32), 0x7FFFFFFF, None, ALU.bitwise_and))
            step(nc.vector.tensor_tensor(decay[:, :], acol[:, :], dts[:, :], ALU.mult))
            step(nc.vector.tensor_scalar(decay[:, :], decay[:, :], -1.0, None, ALU.mult))
            v.sem_inc(dts_done, 1)
            for b in range(B):
                x, y = x1[:, rows(b), :], xn[:, rows(b), :]
                v.wait_ge(x_in[b], 16)
                v.wait_ge(prT_ready, b + 1)
                step(nc.vector.tensor_tensor(x.rearrange("p n d -> p (n d)"), ps_a[:, :], x.rearrange("p n d -> p (n d)"), ALU.add))
                step(nc.vector.tensor_reduce(sums[:, :], x, AX.X, ALU.add))
                step(nc.vector.tensor_scalar(neg_mean[:, :], sums[:, :], -1.0 / D, None, ALU.mult))
                nc.vector.tensor_tensor(y, x, neg_mean[:, :].unsqueeze(2).to_broadcast([P, TPB, D]), ALU.add).then_inc(mid_done, 1)
                v.wait_ge(sq_done, 2 * b + 1)
                step(nc.vector.tensor_reduce(sums[:, :], sq[:, :, :], AX.X, ALU.add))
                nc.vector.tensor_scalar(var[:, 0, :], sums[:, :], 1.0 / D, LN_EPS, ALU.mult, ALU.add).then_inc(var_done, 1)
                v.wait_ge(rstd_done, 2 * b + 1)
                nc.vector.tensor_tensor(y, y, rstd[:, 0, :].unsqueeze(2).to_broadcast([P, TPB, D]), ALU.mult).then_inc(mid_done, 1)
                v.wait_ge(sq_done, 2 * b + 2)
                step(nc.vector.tensor_reduce(sums[:, :], sq[:, :, :], AX.X, ALU.add))
                nc.vector.tensor_scalar(var[:, 1, :], sums[:, :], 1.0 / D, RMS_EPS, ALU.mult, ALU.add).then_inc(var_done, 1)
                v.wait_ge(rstd_done, 2 * b + 2)
                if b:
                    v.wait_ge(uT_ready, b)
                nc.vector.tensor_tensor(u[:, :, :], y, rstd[:, 1, :].unsqueeze(2).to_broadcast([P, TPB, D]), ALU.mult).then_inc(u_done, 1)
            v.wait_ge(a_done, 1)
            for q in range(2):
                v.wait_ge(ud_done, 2 * q + 2)
                nc.vector.tensor_tensor_scan(states[:, q, :], decay[:, 0:1].to_broadcast([P, T]), ud[:, q, :], 0.0,
                                             ALU.mult, ALU.add).then_inc(scan_done, 1)
            v.wait_ge(w_in, 7 * 16)

            def blocks(ap):
                return ap.rearrange("p (n k) -> p n k", k=BLK)

            def quantise(chained, x, out):
                nb = x.shape[1]
                fp4(nc, chained, x, s_[:, 0:nb], rs_[:, 0:nb], v_[:, 0:nb, :], av_[:, 0:nb, :], hi_[:, 0:nb, :], low_[:, 0:nb, :], out)

            quantise(step, blocks(w_gu[:, :, :].rearrange("p j d -> p (j d)")), blocks(wq_gu[:, :, :].rearrange("p j d -> p (j d)")))
            quantise(step, blocks(w_dn[:, :]), blocks(wq_dn[:, :]))
            v.sem_inc(wq_done, 1)
            with v.Fori(0, NCH) as c:
                m = 0

                def in_loop(ins):
                    nonlocal m
                    m += 1
                    ins.then_inc(c_step, 1)
                    v.wait_ge(c_step, c * (2 * FP4_STEPS) + m)

                quantise(in_loop, xn[:, bass.ds(c * TC, TC), :].rearrange("p t (n k) -> p (t n) k", k=BLK),
                         xq[:, :, :].rearrange("p t (n k) -> p (t n) k", k=BLK))
                v.sem_inc(xq_done, 1)
                for t in range(TC):
                    v.wait_ge(sg_done, c * TC + t + 1)
                    nc.vector.tensor_tensor(h[:, t, :], ps_c[:, t % 2 * CH:t % 2 * CH + INNER], sg[:, t % 2, :], ALU.mult).then_inc(h_done, 1)
                v.wait_ge(h_done, c * TC + TC)
                hb = h[:, :, :].rearrange("p t (n k) -> p (t n) k", k=BLK)
                quantise(in_loop, hb, hb)
                v.sem_inc(hq_done, 1)
                v.wait_ge(o_ready, c + 1)
                v.wait_ge(stored, c * 16 + 1)
                nc.vector.tensor_tensor(out_t[:, :, :].rearrange("p t d -> p (t d)"), ps_b[:, 0:CH],
                                        x1[:, bass.ds(c * TC, TC), :].rearrange("p t d -> p (t d)"), ALU.add).then_inc(o_done, 1)

        @block.tensor
        def _(pe):
            for b in range(B):
                pe.wait_ge(pr_done, b + 1)
                if b:
                    pe.wait_ge(mid_done, 2 * b - 1)
                for t in range(TPB):
                    tok = slice(b * T + t * P, b * T + (t + 1) * P)
                    ins = nc.tensor.transpose(ps_a[:, t * P:(t + 1) * P], g.sT[:, tok], g.ident[:, :])
                ins.then_inc(prT_ready, 1)
                if b == 0:
                    pe.wait_ge(c_in, 6 * 16)
                pe.wait_ge(u_done, b + 1)
                if b:
                    pe.wait_ge(uT_done, b)
                for t in range(TPB):
                    ins = nc.tensor.transpose(ps_b[:, t * P:(t + 1) * P], u[:, t, :], g.ident[:, :])
                ins.then_inc(uT_ready, 1)
                pe.wait_ge(uT_done, b + 1)
                if b >= 2:
                    pe.wait_ge(ud_done, b - 1)
                r = slice(b % 2 * S, (b % 2 + 1) * S)
                for k in range(HALF):
                    cols = slice(k * CH, (k + 1) * CH)
                    ins = nc.tensor.matmul(ps_c[r, cols], bmat[:, :], uT[:, cols], start=True, stop=True)
                ins.then_inc(up_ready, 1)
            pe.wait_ge(mid_done, 2 * B)
            for q in range(B):
                pe.wait_ge(scan_done, q // 2 + 1)
                if q >= 2:
                    pe.wait_ge(y_done, 2 * (q - 1))
                r = slice(q % 2 * S, (q % 2 + 1) * S)
                for k in range(HALF):
                    cols = slice(k * CH, (k + 1) * CH)
                    ins = nc.tensor.matmul((ps_a, ps_b)[q % 2][:, cols], cmat[r, :], states[r, q // 2, cols], start=True, stop=True)
                ins.then_inc(y_ready, 1)
            pe.wait_ge(wq_done, 1)
            pe.wait_ge(y_done, 2 * B)
            for k in range(2):
                for j, (lo, n) in enumerate(IB):
                    nc.tensor.transpose(ps_d[k][:, lo:lo + n], wq_gu[0:n, 3 * k + j, :], g.ident[0:n, 0:n])
            for j, (lo, n) in enumerate(IB):
                ins = nc.tensor.transpose(ps_a[0:n, j * P:(j + 1) * P], wq_dn[:, lo:lo + n], g.ident[:, :])
            ins.then_inc(wT_ready, 1)
            pe.wait_ge(wT_done, 1)
            with pe.Fori(0, NCH) as c:
                pe.wait_ge(xq_done, c + 1)
                for t in range(TC):
                    ins = nc.tensor.transpose(ps_a[:, t * P:(t + 1) * P], xq[:, t, :], g.ident[:, :])
                ins.then_inc(xqT_ready, 1)
                pe.wait_ge(xqT_done, c + 1)
                for t in range(TC):
                    if t >= 2:
                        pe.wait_ge(h_done, c * TC + t - 1)
                    tok = slice(t * P, (t + 1) * P)
                    nc.tensor.matmul(ps_d[t % 2][:, 0:INNER], xqT[:, tok], wT_gu[:, 0:INNER], start=True, stop=True)
                    nc.tensor.matmul(ps_c[:, t % 2 * CH:t % 2 * CH + INNER], xqT[:, tok], wT_gu[:, INNER:2 * INNER],
                                     start=True, stop=True).then_inc(gu_ready, 1)
                pe.wait_ge(hq_done, c + 1)
                for j, (lo, n) in enumerate(IB):
                    dst = (ps_b[0:n, 0:CH], ps_b[0:n, CH:T], ps_a[0:n, CH:T])[j]
                    for t in range(TC):
                        ins = nc.tensor.transpose(dst[:, t * P:(t + 1) * P], h[:, t, lo:lo + n], g.ident[:, :])
                ins.then_inc(hT_ready, 1)
                pe.wait_ge(hT_done, c + 1)
                for j, (lo, n) in enumerate(IB):
                    ins = nc.tensor.matmul(ps_a[:, 0:CH], wT_dn[0:n, j, :], hqT[0:n, j, :], start=j == 0, stop=j == 2)
                ins.then_inc(dn_ready, 1)
                pe.wait_ge(pr2_done, c + 1)
                for t in range(TC):
                    ins = nc.tensor.transpose(ps_b[:, t * P:(t + 1) * P], pr2[:, t * P:(t + 1) * P], g.ident[:, :])
                ins.then_inc(o_ready, 1)


class Shared:

    def __init__(self, nc):
        self.nc = nc

    def scope(self, ctx):
        nc = self.nc

        def sb(name, shape, dt):
            return ctx.enter_context(nc.sbuf_tensor(name, shape, dt))

        def pb(name, shape):
            return ctx.enter_context(nc.psum_tensor(name, shape, F32))

        def sem(name):
            return ctx.enter_context(nc.semaphore(name))

        return sb, pb, sem


def program(nc, args, out):
    g = Shared(nc)
    g.inp = args
    g.out = out
    with ExitStack() as ctx:
        sb, pb, sem = g.scope(ctx)
        g.ident = sb("ident", [P, P], F32)
        g.gT = sb("gT", [P, NT], F32)
        g.sT = sb("sT", [P, NT], F32)
        with ExitStack() as layer0:
            sb0, _, _ = g.scope(layer0)
            g.xh = sb0("xh", [P, NT], F32R)
            g.xl = sb0("xl", [P, NT], F32R)
            with ExitStack() as ffn:
                sb1, _, _ = g.scope(ffn)
                g.combT = sb1("combT", [2 * NE, NT], F32R)
                with ExitStack() as stage:
                    layer0_norm_and_router(nc, stage, g)
                with ExitStack() as stage:
                    layer0_experts(nc, stage, g)
            with ExitStack() as stage:
                layer0_attention(nc, stage, g)
        with ExitStack() as stage:
            layer1(nc, stage, g)






def layouts(np, a):
    c = np.ascontiguousarray
    up = np.concatenate([a["L0_ffn_w_fc"], a["L0_ffn_shared_fc"][None]])
    dn = np.concatenate([a["L0_ffn_w_proj"], a["L0_ffn_shared_proj"][None]])
    wq = a["L0_attn_W_qkv"].reshape(D, PAIRS, 2 * DH, 3)
    sel = np.zeros((2 * NE, NE, P), np.float32)
    for e in range(NE):
        sel[e, e] = sel[NE + e, e] = 1.0
    mask = np.zeros((2, 8, 4, P), np.float32)
    for x in range(2):
        for j in range(4):
            mask[x, 4 * x + j, j] = -1.0
    return {
        "X": c(a["L0_attn_X"]),
        "ident_d": np.eye(P, dtype=np.float32),
        "iota8_d": c(np.broadcast_to(np.arange(E, dtype=np.float32), (P, E))),
        "router_wT": c(a["L0_ffn_router_w"].T),
        "upT": c(up.transpose(0, 2, 1)),
        "dnT": c(dn.transpose(0, 2, 1).reshape(NE, FT, P, D).transpose(0, 2, 1, 3).reshape(NE, P, FF)),
        "sel_d": sel.reshape(2 * NE, NE * P),
        "qkv_d": c(wq.transpose(0, 1, 3, 2)),
        "wout_d": c(a["L0_attn_W_out"].reshape(PAIRS, P, D).transpose(1, 0, 2)),
        "mask_d": c(mask.transpose(1, 0, 2, 3).reshape(8, 2, CH)),
        "dt_d": c(np.tile(a["L1_attn_dt"], 2).reshape(P, 1)),
        "A_d": c(np.tile(a["L1_attn_A"], 2).reshape(P, 1)),
        "Bmat_d": c(a["L1_attn_Bmat"]),
        "C_d": c(np.concatenate([a["L1_attn_C"]] * 2)),
        "D_d": c(a["L1_attn_D"].reshape(D, 1)),
        "norm_w_d": c(a["L1_attn_norm_w"].reshape(D, 1)),
        "w_gate_d": c(a["L1_ffn_w_gate"]),
        "w_up_d": c(a["L1_ffn_w_up"]),
        "w_down_d": c(a["L1_ffn_w_down"]),
    }


def kernel(**inputs):
    import numpy as np
    import concourse.bacc as bacc
    from concourse.bass_utils import run_bass_kernel_spmd as run

    nc = bacc.Bacc("TRN2", target_bir_lowering=False, num_devices=1)
    arrays, args = {}, {}
    for name, value in layouts(np, {k: np.asarray(v) for k, v in inputs.items()}).items():
        arrays[f"in_{name}"] = value
        args[name] = nc.dram_tensor(f"in_{name}", value.shape, mybir.dt.from_np(value.dtype), kind="ExternalInput").ap()
    out = nc.dram_tensor("out_x", (B, T, D), F32, kind="ExternalOutput").ap()
    program(nc, args, out)
    r = run(nc, [arrays], core_ids=[0])
    return r.results[0]["out_x"]
```
